# Optimizing a Trainium2 kernel written in Bass

```python
import numpy as np
import jax
import jax.numpy as jnp

def _softmax(x, axis=-1):
    return jax.nn.softmax(x, axis=axis)

def _gelu(x):
    return jax.nn.gelu(x, approximate=True)

def _silu(x):
    return jax.nn.silu(x)

def _sigmoid(x):
    return jax.nn.sigmoid(x)

def _layernorm(x, axis=-1, eps=1e-05):
    m = jnp.mean(x, axis=axis, keepdims=True)
    v = jnp.var(x, axis=axis, keepdims=True)
    return (x - m) / jnp.sqrt(v + eps)

def _scatter_add(tgt, idx, src, axis=0):
    return tgt.at[idx].add(src)

def _segment_sum(src, seg, n):
    return jax.ops.segment_sum(src, seg, n)
kernel_name = 'mk_gnn_resnorm_d1_gnn_r8_8e2565'

def setup_inputs(seed: int=0):
    np.random.seed(seed)
    _w = jnp.asarray

    def _rec_inputs():
        import jax
        import jax.numpy as jnp
        _gk = jax.random.key(seed)
        x = -0.0002928 + 1 * jax.random.normal(jax.random.fold_in(_gk, 1), (4096, 128), jnp.float32)
        src = jax.random.randint(jax.random.fold_in(_gk, 2), (131072,), 0, 4096, jnp.int32)
        dst = jax.random.randint(jax.random.fold_in(_gk, 3), (131072,), 0, 4096, jnp.int32)
        _o = jnp.argsort(dst, stable=True)
        src = src[_o]
        dst = dst[_o]
        return (x, src, dst)
    x, src, dst = _rec_inputs()

    def _L0_gnn_setup():
        import jax, jax.numpy as jnp
        import numpy as np
        N = 4096
        D = 16
        C = 128
        H = 128

        def _lstm_last(seq, wih, whh, bih, bhh):
            n = seq.shape[1]
            h0 = jnp.zeros((n, wih.shape[0] // 4), seq.dtype)
            b = bih + bhh

            def step(carry, x_t):
                h, c = carry
                g = x_t @ wih.T + h @ whh.T + b
                i, f, gg, o = jnp.split(g, 4, axis=-1)
                c = jax.nn.sigmoid(f) * c + jax.nn.sigmoid(i) * jnp.tanh(gg)
                h = jax.nn.sigmoid(o) * jnp.tanh(c)
                return ((h, c), None)
            (h, _), _ = jax.lax.scan(step, (h0, h0), seq)
            return h

        def _sage_conv(x, src, wih, whh, bih, bhh, wl, bl, wr):
            n, c = x.shape
            d = src.shape[0] // n
            msgs = x[src].reshape(n, d, c)
            aggr = _lstm_last(jnp.swapaxes(msgs, 0, 1), wih, whh, bih, bhh)
            return aggr @ wl.T + bl + x @ wr.T
        key = jax.random.key(seed)
        ks = jax.random.split(key, 20)
        x = jax.random.normal(ks[0], (N, C), dtype=jnp.float32)
        src = jax.random.randint(ks[1], (N * D,), 0, N, dtype=jnp.int32)
        dst = jnp.repeat(jnp.arange(N, dtype=jnp.int32), D)
        edge_index = jnp.stack([src, dst])
        s = 1.0 / np.sqrt(C)

        def mat(k, o, i):
            return jax.random.uniform(k, (o, i), jnp.float32, -s, s)

        def vec(k, o):
            return jax.random.uniform(k, (o,), jnp.float32, -s, s)
        inp = {'x': x, 'edge_index': edge_index}
        for k0, base in [(2, 'conv1'), (10, 'conv2')]:
            inp[f'{base}_wih'] = mat(ks[k0 + 0], 4 * C, C)
            inp[f'{base}_whh'] = mat(ks[k0 + 1], 4 * C, C)
            inp[f'{base}_bih'] = vec(ks[k0 + 2], 4 * C)
            inp[f'{base}_bhh'] = vec(ks[k0 + 3], 4 * C)
            inp[f'{base}_wl'] = mat(ks[k0 + 4], H, C)
            inp[f'{base}_bl'] = vec(ks[k0 + 5], H)
            inp[f'{base}_wr'] = mat(ks[k0 + 6], H, C)
        return inp
    _L0_gnn_all = _L0_gnn_setup()
    _L0_gnn_in = {k: v for k, v in _L0_gnn_all.items() if k in ('conv1_wih', 'conv1_whh', 'conv1_bih', 'conv1_bhh', 'conv1_wl', 'conv1_bl', 'conv1_wr', 'conv2_wih', 'conv2_whh', 'conv2_bih', 'conv2_bhh', 'conv2_wl', 'conv2_bl', 'conv2_wr')}
    del _L0_gnn_all
    return {'x': x, 'src': src, 'dst': dst, 'L0_gnn_conv1_wih': _L0_gnn_in['conv1_wih'], 'L0_gnn_conv1_whh': _L0_gnn_in['conv1_whh'], 'L0_gnn_conv1_bih': _L0_gnn_in['conv1_bih'], 'L0_gnn_conv1_bhh': _L0_gnn_in['conv1_bhh'], 'L0_gnn_conv1_wl': _L0_gnn_in['conv1_wl'], 'L0_gnn_conv1_bl': _L0_gnn_in['conv1_bl'], 'L0_gnn_conv1_wr': _L0_gnn_in['conv1_wr'], 'L0_gnn_conv2_wih': _L0_gnn_in['conv2_wih'], 'L0_gnn_conv2_whh': _L0_gnn_in['conv2_whh'], 'L0_gnn_conv2_bih': _L0_gnn_in['conv2_bih'], 'L0_gnn_conv2_bhh': _L0_gnn_in['conv2_bhh'], 'L0_gnn_conv2_wl': _L0_gnn_in['conv2_wl'], 'L0_gnn_conv2_bl': _L0_gnn_in['conv2_bl'], 'L0_gnn_conv2_wr': _L0_gnn_in['conv2_wr']}

def reference(x, src, dst, L0_gnn_conv1_wih, L0_gnn_conv1_whh, L0_gnn_conv1_bih, L0_gnn_conv1_bhh, L0_gnn_conv1_wl, L0_gnn_conv1_bl, L0_gnn_conv1_wr, L0_gnn_conv2_wih, L0_gnn_conv2_whh, L0_gnn_conv2_bih, L0_gnn_conv2_bhh, L0_gnn_conv2_wl, L0_gnn_conv2_bl, L0_gnn_conv2_wr):
    import jax
    import jax.numpy as jnp

    def _L0_gnn_ref(x, edge_index, conv1_wih, conv1_whh, conv1_bih, conv1_bhh, conv1_wl, conv1_bl, conv1_wr, conv2_wih, conv2_whh, conv2_bih, conv2_bhh, conv2_wl, conv2_bl, conv2_wr):
        import jax, jax.numpy as jnp
        import numpy as np
        N = 4096
        D = 16
        C = 128
        H = 128

        def _lstm_last(seq, wih, whh, bih, bhh):
            n = seq.shape[1]
            h0 = jnp.zeros((n, wih.shape[0] // 4), seq.dtype)
            b = bih + bhh

            def step(carry, x_t):
                h, c = carry
                g = x_t @ wih.T + h @ whh.T + b
                i, f, gg, o = jnp.split(g, 4, axis=-1)
                c = jax.nn.sigmoid(f) * c + jax.nn.sigmoid(i) * jnp.tanh(gg)
                h = jax.nn.sigmoid(o) * jnp.tanh(c)
                return ((h, c), None)
            (h, _), _ = jax.lax.scan(step, (h0, h0), seq)
            return h

        def _sage_conv(x, src, wih, whh, bih, bhh, wl, bl, wr):
            n, c = x.shape
            d = src.shape[0] // n
            msgs = x[src].reshape(n, d, c)
            aggr = _lstm_last(jnp.swapaxes(msgs, 0, 1), wih, whh, bih, bhh)
            return aggr @ wl.T + bl + x @ wr.T
        src = edge_index[0]
        h = _sage_conv(x, src, conv1_wih, conv1_whh, conv1_bih, conv1_bhh, conv1_wl, conv1_bl, conv1_wr)
        h = jax.nn.relu(h)
        out = _sage_conv(h, src, conv2_wih, conv2_whh, conv2_bih, conv2_bhh, conv2_wl, conv2_bl, conv2_wr)
        return out
    edge_index = jnp.stack([src, dst])
    x = _layernorm(x + _L0_gnn_ref(x, edge_index, L0_gnn_conv1_wih, L0_gnn_conv1_whh, L0_gnn_conv1_bih, L0_gnn_conv1_bhh, L0_gnn_conv1_wl, L0_gnn_conv1_bl, L0_gnn_conv1_wr, L0_gnn_conv2_wih, L0_gnn_conv2_whh, L0_gnn_conv2_bih, L0_gnn_conv2_bhh, L0_gnn_conv2_wl, L0_gnn_conv2_bl, L0_gnn_conv2_wr), axis=-1)
    return x

_drawn_inputs = setup_inputs


def setup_inputs(seed=0):
    import zlib

    import numpy as np

    out = dict(_drawn_inputs(seed))
    spreads = {}
    factors = {'L0_gnn_conv1_whh': 8.0,
     'L0_gnn_conv1_bih': 8.0,
     'L0_gnn_conv1_bhh': 8.0,
     'L0_gnn_conv2_whh': 4.436,
     'L0_gnn_conv2_bih': 3.63,
     'L0_gnn_conv2_bhh': 4.083}
    for name, (base, spread) in spreads.items():
        noise = np.random.default_rng([zlib.crc32(name.encode()), seed]).standard_normal(out[name].shape)
        drawn = base * np.exp(spread * noise) if base else spread * noise
        out[name] = jnp.asarray(drawn.astype(out[name].dtype))
    for name, factor in factors.items():
        out[name] = (out[name] * factor).astype(out[name].dtype)
    return out
```

```python
import concourse.bass as bass
from concourse import mybir
from contextlib import ExitStack


def sage_lstm_resnorm_kernel(nc, x, src, layers, table, out):
    fp32 = mybir.dt.float32
    fp16 = mybir.dt.float16
    i32 = mybir.dt.int32
    u32 = mybir.dt.uint32
    ALU = mybir.AluOpType
    ACT = mybir.ActivationFunctionType

    P = 128
    N, C = x.shape
    DEG = src.shape[0] // N
    NQ = 4
    GW = NQ * C
    TILE = 512
    BPT = TILE // P
    NBLK = N // P
    NT = N // TILE
    LAYERS = 2
    ROWSLOTS = 4
    W_SCALE = 2.0 ** 4
    H_SCALE = 2.0 ** 8
    Z_SCALE = W_SCALE * H_SCALE
    GATE = [1, 0, 3, 2]
    EPS = 1e-5
    TILES = DEG * NT

    ctx = ExitStack()
    with ctx:
        def sb(name, shape, dt=fp32):
            return ctx.enter_context(nc.sbuf_tensor(name, shape, dt))

        def sem(name):
            return ctx.enter_context(nc.semaphore(name))

        idx = sb("idx", [P, NBLK, DEG], i32)
        stage = sb("stage", [P, NT, BPT], i32)
        ident = sb("ident", [P, P])
        xT = sb("xT", [P, N])
        h1T = sb("h1T", [P, N])
        h32 = sb("h32", [P, N])
        h_hi = sb("h_hi", [P, N], fp16)
        h_lo = sb("h_lo", [P, N], fp16)
        rows = sb("rows", [P, ROWSLOTS, BPT, GW])
        cg = sb("cg", [P, NT + 2, TILE])
        sig = sb("sig", [P, 2, 3, TILE])
        prod = sb("prod", [P, 2, 2, TILE])
        tanc = sb("tanc", [P, 2, TILE])
        w_in = sb("w_in", [P, LAYERS, 2 * NQ + 2, C])
        b_in = sb("b_in", [P, LAYERS, 2, GW])
        b_sum = sb("b_sum", [P, LAYERS, GW])
        bias = sb("bias", [P, LAYERS, GW])
        wihT = sb("wihT", [P, LAYERS, GW])
        w_hi = sb("w_hi", [P, LAYERS, GW], fp16)
        w_lo = sb("w_lo", [P, LAYERS, GW], fp16)
        whh32 = sb("whh32", [P, LAYERS, GW])
        wlrT = sb("wlrT", [P, LAYERS, 2, C])
        bl1 = sb("bl1", [P, 1])
        bl2 = sb("bl2", [P, C])
        stats = sb("stats", [P, NBLK, 6])
        mv = sb("mv", [P, NBLK, 2])
        rstd = sb("rstd", [P, NBLK])
        epst = sb("epst", [P, 1])
        ps = ctx.enter_context(nc.psum_tensor("ps", [P, 8, TILE], fp32))

        x_in = h32[:, :].rearrange("p (b c) -> p b c", c=C)
        x_res = xT[:, :].rearrange("p (b c) -> p b c", c=C)
        y = h1T[:, :].rearrange("p (b c) -> p b c", c=C)

        x_loaded = [sem(f"x_loaded{k}") for k in range(NT)]
        idx_loaded = sem("idx_loaded")
        w_loaded = sem("w_loaded")
        xres_loaded = sem("xres_loaded")
        ident_zero = sem("ident_zero")
        ident_ready = sem("ident_ready")
        w_transposed = sem("w_transposed")
        w_ready = sem("w_ready")
        xT_psum = sem("xT_psum")
        xT_ready = sem("xT_ready")
        table_psum = sem("table_psum")
        table_evac = sem("table_evac")
        table_stored = [sem(f"table_stored{k}") for k in range(ROWSLOTS)]
        staged = sem("staged")
        gathered = [sem(f"gathered{k}") for k in range(ROWSLOTS)]
        gather_turn = sem("gather_turn")
        rows_used = sem("rows_used")
        gates_ready = sem("gates_ready")
        acts_ready = sem("acts_ready")
        prod_ready = sem("prod_ready")
        c_ready = sem("c_ready")
        tanc_ready = sem("tanc_ready")
        h32_ready = sem("h32_ready")
        hi_ready = sem("hi_ready")
        h_ready = sem("h_ready")
        lin_ready = sem("lin_ready")
        h1_ready = sem("h1_ready")
        out_psum = sem("out_psum")
        y_sum = sem("y_sum")
        b_summed = sem("b_summed")
        bias_ready = sem("bias_ready")
        w_split = sem("w_split")
        xres_ready = sem("xres_ready")
        stats_ready = sem("stats_ready")
        mv_ready = sem("mv_ready")
        std_ready = sem("std_ready")
        rstd_ready = sem("rstd_ready")
        y_ready = sem("y_ready")
        stored = sem("stored")
        eps_ready = sem("eps_ready")

        block = ctx.enter_context(nc.Block())

        def blk(b):
            return slice(b * P, (b + 1) * P)

        def tl(j):
            return slice(j * TILE, (j + 1) * TILE)

        W_LOADS = 6 * LAYERS + 2
        W_GROUPS = 3
        W_READY = 3 * LAYERS

        @block.sync
        def _(sp):
            for k in range(NT):
                sp.dma_start(x_in[:, k * BPT:(k + 1) * BPT, :],
                             x[k * TILE:(k + 1) * TILE, :].rearrange("(b p) c -> p b c", p=P)
                             ).then_inc(x_loaded[k], 16)
            sp.dma_start(idx[:, :, :], src.rearrange("(b p t) -> p b t", p=P, t=DEG)).then_inc(idx_loaded, 16)
            for layer in range(LAYERS):
                for k in range(NT):
                    n = layer * NT + k
                    sp.wait_ge(table_evac, (n + 1) * BPT)
                    sp.dma_start(table[layer][k * TILE:(k + 1) * TILE, :].rearrange("(b p) g -> p b g", p=P),
                                 rows[:, n % ROWSLOTS, :, :]).then_inc(table_stored[n % ROWSLOTS], 16)
                if layer == 1:
                    sp.wait_ge(h1_ready, NT)
                    sp.dma_start(x_res, x.rearrange("(b p) c -> p b c", p=P)).then_inc(xres_loaded, 16)
            for k in range(NT):
                sp.wait_ge(y_ready, (k + 1) * BPT)
                sp.dma_start(out[k * TILE:(k + 1) * TILE, :].rearrange("(b p) c -> p b c", p=P),
                             y[:, k * BPT:(k + 1) * BPT, :]).then_inc(stored, 16)
            sp.wait_ge(stored, 16 * NT)

        @block.gpsimd
        def _(pool):
            nc.gpsimd.memset(ident[:, :], 0.0).then_inc(ident_zero, 1)
            pool.wait_ge(ident_zero, 1)
            nc.gpsimd.affine_select(out=ident[:, :], in_=ident[:, :], compare_op=ALU.not_equal, fill=1.0,
                                    base=0, pattern=[[-1, P]], channel_multiplier=1).then_inc(ident_ready, 1)
            pool.wait_ge(idx_loaded, 16)

            def gather_step(layer, t, first):
                for j in range(NT):
                    tile = layer * TILES + t * NT + j
                    slot = j % ROWSLOTS
                    if not (first and layer == 0 and j < ROWSLOTS):
                        pool.wait_ge(rows_used, tile - ROWSLOTS + 1)
                    nc.gpsimd.tensor_copy(stage[:, j, :], idx[:, j * BPT:(j + 1) * BPT, t]
                                          ).then_inc(staged, 1)
                    pool.wait_ge(staged, tile + 1)
                    pool.sem_inc(gather_turn, 1)
                    for b in range(BPT):
                        nc.gpsimd.indirect_dma_start(
                            rows[:, slot, b, :], None, table[layer],
                            bass.IndirectOffsetOnAxis(stage[:, j, b:b + 1].bitcast(u32), 0)
                        ).then_inc(gathered[slot], 16)

            for layer in range(LAYERS):
                for k in range(ROWSLOTS):
                    pool.wait_ge(table_stored[k], 16 * (layer + 1) * NT // ROWSLOTS)
                gather_step(layer, 0, True)
                with pool.Fori(1, DEG) as t:
                    gather_step(layer, t, False)

        @block.tensor
        def _(pe):
            pe.wait_ge(ident_ready, 1)
            pe.wait_ge(w_loaded, 16 * W_LOADS)
            n = 0
            for layer in range(LAYERS):
                for group in range(3):
                    if n >= 2:
                        pe.wait_ge(w_ready, n - 1)
                    cols = [2 * NQ, 2 * NQ + 1] if group == 2 else [group * NQ + q for q in GATE]
                    for k, w in enumerate(cols):
                        last = nc.tensor.transpose(ps[:, n % 2, blk(k)], w_in[:, layer, w, :], ident[:, :])
                    last.then_inc(w_transposed, 1)
                    n += 1
            for k in range(NT):
                pe.wait_ge(x_loaded[k], 16)
                if k >= 2:
                    pe.wait_ge(xT_ready, k - 1)
                for b in range(BPT):
                    last = nc.tensor.transpose(ps[:, 2 + k % 2, blk(b)], x_in[:, k * BPT + b, :], ident[:, :])
                last.then_inc(xT_psum, 1)
            pe.wait_ge(w_ready, W_READY)
            pe.wait_ge(w_split, 2 * LAYERS)
            pe.wait_ge(bias_ready, 1)

            def table_rows(layer, inT):
                for b in range(NBLK):
                    n = layer * NBLK + b
                    if layer == 0 and b % BPT == 0:
                        pe.wait_ge(xT_ready, b // BPT + 1)
                    if layer == 1 and b % BPT == 0:
                        pe.wait_ge(h1_ready, b // BPT + 1)
                    if n >= 4:
                        pe.wait_ge(table_evac, n - 3)
                    nc.tensor.matmul(ps[:, 4 + n % 4, :], inT[:, blk(b)], wihT[:, layer, :],
                                     start=True, stop=True).then_inc(table_psum, 1)

            def gates_step(layer, t, first):
                for j in range(NT):
                    tile = layer * TILES + t * NT + j
                    bank = j % 2 * NQ
                    slot = j % ROWSLOTS
                    pe.wait_ge(gathered[slot], (16 * BPT) * (layer * TILES // ROWSLOTS + t * (NT // ROWSLOTS)
                                                            + j // ROWSLOTS + 1))
                    if not (first and layer == 0 and j < 2):
                        pe.wait_ge(acts_ready, tile - 1)
                    for q in range(NQ):
                        for b in range(BPT):
                            last = nc.tensor.matmul(ps[:, bank + q, blk(b)], rows[:, slot, b, blk(q)], ident[:, :],
                                                    start=b == 0, stop=first and b == BPT - 1,
                                                    is_transpose=True, skip_group_check=True)
                    last.then_inc(rows_used, 1)
                    if first:
                        continue
                    pe.wait_ge(h_ready, tile - NT + 1)
                    for q in range(NQ):
                        for k, (w, h) in enumerate(((w_hi, h_hi), (w_lo, h_hi), (w_hi, h_lo))):
                            last = nc.tensor.matmul(ps[:, bank + q, :], w[:, layer, blk(q)], h[:, tl(j)],
                                                    start=False, stop=k == 2, skip_group_check=True)
                    last.then_inc(gates_ready, 1)

            def all_steps(layer):
                gates_step(layer, 0, True)
                with pe.Fori(1, DEG) as t:
                    gates_step(layer, t, False)

            table_rows(0, xT)
            pe.wait_ge(table_evac, NBLK)
            all_steps(0)
            for j in range(NT):
                pe.wait_ge(h32_ready, TILES - NT + j + 1)
                pe.wait_ge(acts_ready, TILES)
                if j >= 4:
                    pe.wait_ge(h1_ready, j - 3)
                nc.tensor.matmul(ps[:, j % 4, :], wlrT[:, 0, 1, :], xT[:, tl(j)], start=True, stop=False)
                nc.tensor.matmul(ps[:, j % 4, :], wlrT[:, 0, 0, :], h32[:, tl(j)], start=False, stop=True
                                 ).then_inc(lin_ready, 1)
            table_rows(1, h1T)
            pe.wait_ge(table_evac, 2 * NBLK)
            all_steps(1)
            pe.wait_ge(acts_ready, 2 * TILES)
            for k in range(NT):
                pe.wait_ge(h32_ready, 2 * TILES - NT + k + 1)
                for b in range(BPT):
                    n = k * BPT + b
                    nc.tensor.matmul(ps[:, k, blk(b)], h1T[:, blk(n)], wlrT[:, 1, 1, :],
                                     start=True, stop=False, skip_group_check=True)
                    last = nc.tensor.matmul(ps[:, k, blk(b)], h32[:, blk(n)], wlrT[:, 1, 0, :],
                                            start=False, stop=True, skip_group_check=True)
                last.then_inc(out_psum, 1)

        @block.scalar
        def _(act):
            for layer in range(LAYERS):
                wih, whh, bih, bhh, wl, bl, wr = layers[layer]
                act.dma_start(w_in[:, layer, 0:NQ, :], wih.rearrange("(q p) c -> p q c", p=P)).then_inc(w_loaded, 16)
                act.dma_start(w_in[:, layer, NQ:2 * NQ, :], whh.rearrange("(q p) c -> p q c", p=P)
                              ).then_inc(w_loaded, 16)
                act.dma_start(w_in[:, layer, 2 * NQ, :], wl).then_inc(w_loaded, 16)
                act.dma_start(w_in[:, layer, 2 * NQ + 1, :], wr).then_inc(w_loaded, 16)
                for k, v in enumerate((bih, bhh)):
                    act.dma_start(b_in[:, layer, k, :], v.rearrange("(o g) -> o g", o=1).to_broadcast([P, GW])
                                  ).then_inc(w_loaded, 16)
            act.dma_start(bl1[:, :], layers[0][5].rearrange("(c o) -> c o", o=1)).then_inc(w_loaded, 16)
            act.dma_start(bl2[:, :], layers[1][5].rearrange("(o c) -> o c", o=1).to_broadcast([P, C])
                          ).then_inc(w_loaded, 16)
            for k in range(NT):
                act.wait_ge(xT_psum, k + 1)
                nc.scalar.copy(xT[:, tl(k)], ps[:, 2 + k % 2, :]).then_inc(xT_ready, 1)

            def act_step(layer, t, first):
                for j in range(NT):
                    tile = layer * TILES + t * NT + j
                    bank = j % 2 * NQ
                    if first:
                        act.wait_ge(rows_used, tile + 1)
                    else:
                        act.wait_ge(gates_ready, tile + 1 - NT * (layer + 1))
                    if not (first and layer == 0 and j < 2):
                        act.wait_ge(h32_ready, tile - 1)
                    nc.scalar.activation(sig[:, j % 2, :, :], ps[:, bank:bank + 3, :], ACT.Sigmoid,
                                         scale=1.0 / Z_SCALE)
                    nc.scalar.activation(cg[:, NT + j % 2, :], ps[:, bank + 3, :], ACT.Tanh,
                                         scale=1.0 / Z_SCALE).then_inc(acts_ready, 1)
                    if not (first and j == 0):
                        tanh_c(tile - 1, (j - 1) % NT)

            def tanh_c(tile, j):
                act.wait_ge(c_ready, tile + 1)
                nc.scalar.activation(tanc[:, j % 2, :], cg[:, j, :], ACT.Tanh).then_inc(tanc_ready, 1)

            def all_steps(layer):
                act_step(layer, 0, True)
                with act.Fori(1, DEG) as t:
                    act_step(layer, t, False)

            all_steps(0)
            tanh_c(TILES - 1, NT - 1)
            act.wait_ge(w_loaded, 16 * W_LOADS)
            for j in range(NT):
                act.wait_ge(lin_ready, j + 1)
                nc.scalar.activation(h1T[:, tl(j)], ps[:, j % 4, :], ACT.Relu, bias=bl1[:, :]
                                     ).then_inc(h1_ready, 1)
            all_steps(1)
            tanh_c(2 * TILES - 1, NT - 1)
            act.wait_ge(mv_ready, NBLK)
            act.wait_ge(eps_ready, 1)
            nc.scalar.activation(rstd[:, :], mv[:, :, 1], ACT.Sqrt, bias=epst[:, :]).then_inc(std_ready, 1)

        @block.vector
        def _(dve):
            nc.vector.memset(epst[:, :], EPS).then_inc(eps_ready, 1)
            dve.wait_ge(w_loaded, 16 * W_LOADS)
            for layer in range(LAYERS):
                for k, q in enumerate(GATE):
                    nc.vector.tensor_tensor(b_sum[:, layer, blk(k)], b_in[:, layer, 0, blk(q)],
                                            b_in[:, layer, 1, blk(q)], ALU.add).then_inc(b_summed, 1)
            dve.wait_ge(b_summed, LAYERS * NQ)
            nc.vector.tensor_scalar(bias[:, :, :], b_sum[:, :, :], Z_SCALE, None, ALU.mult).then_inc(bias_ready, 1)
            dve.wait_ge(bias_ready, 1)
            for layer in range(LAYERS):
                n = layer * W_GROUPS
                dve.wait_ge(w_transposed, n + 1)
                nc.vector.tensor_scalar(wihT[:, layer, :], ps[:, n % 2, :], Z_SCALE, None, ALU.mult
                                        ).then_inc(w_ready, 1)
                dve.wait_ge(w_transposed, n + 2)
                nc.vector.tensor_scalar(whh32[:, layer, :], ps[:, (n + 1) % 2, :], W_SCALE, None, ALU.mult
                                        ).then_inc(w_ready, 1)
                dve.wait_ge(w_transposed, n + 3)
                dve.wait_ge(w_ready, n + 2)
                nc.vector.tensor_copy(w_hi[:, layer, :], whh32[:, layer, :]).then_inc(w_split, 1)
                nc.vector.tensor_scalar(wlrT[:, layer, 0, :], ps[:, n % 2, blk(0)], 1.0 / H_SCALE, None, ALU.mult)
                nc.vector.tensor_copy(wlrT[:, layer, 1, :], ps[:, n % 2, blk(1)]).then_inc(w_ready, 1)
                dve.wait_ge(w_split, 2 * layer + 1)
                nc.vector.tensor_tensor(w_lo[:, layer, :], whh32[:, layer, :], w_hi[:, layer, :], ALU.subtract
                                        ).then_inc(w_split, 1)

            def table_rows(layer):
                for b in range(NBLK):
                    n = layer * NBLK + b
                    k = n // BPT
                    if b % BPT == 0 and k >= ROWSLOTS:
                        dve.wait_ge(table_stored[k % ROWSLOTS], 16 * (k // ROWSLOTS))
                    dve.wait_ge(table_psum, n + 1)
                    nc.vector.tensor_tensor(rows[:, k % ROWSLOTS, n % BPT, :], ps[:, 4 + n % 4, :],
                                            bias[:, layer, :], ALU.add).then_inc(table_evac, 1)

            def h_start(tile, j):
                dve.wait_ge(tanc_ready, tile + 1)
                nc.vector.scalar_tensor_tensor(h32[:, tl(j)], sig[:, j % 2, 2, :], H_SCALE, tanc[:, j % 2, :],
                                               ALU.mult, ALU.mult).then_inc(h32_ready, 1)

            def h_split(tile, j):
                dve.wait_ge(h32_ready, tile + 1)
                nc.vector.tensor_copy(h_hi[:, tl(j)], h32[:, tl(j)]).then_inc(hi_ready, 1)
                dve.wait_ge(hi_ready, tile + 1)
                nc.vector.tensor_tensor(h_lo[:, tl(j)], h32[:, tl(j)], h_hi[:, tl(j)], ALU.subtract
                                        ).then_inc(h_ready, 1)

            def state_step(layer, t, first):
                for j in range(NT):
                    tile = layer * TILES + t * NT + j
                    g = NT + j % 2
                    dve.wait_ge(acts_ready, tile + 1)
                    if first:
                        nc.vector.tensor_tensor(cg[:, j, :], sig[:, j % 2, 1, :], cg[:, g, :], ALU.mult
                                                ).then_inc(c_ready, 1)
                        if j > 0:
                            h_start(tile - 1, j - 1)
                    else:
                        nc.vector.tensor_tensor(prod[:, j % 2, :, :], sig[:, j % 2, 0:2, :],
                                                cg[:, j:g + 1:g - j, :], ALU.mult).then_inc(prod_ready, 1)
                        h_start(tile - 1, (j - 1) % NT)
                        dve.wait_ge(prod_ready, tile + 1 - NT * (layer + 1))
                        nc.vector.tensor_tensor(cg[:, j, :], prod[:, j % 2, 0, :], prod[:, j % 2, 1, :], ALU.add
                                                ).then_inc(c_ready, 1)
                    if not (first and j == 0):
                        h_split(tile - 1, (j - 1) % NT)

            def all_steps(layer):
                state_step(layer, 0, True)
                with dve.Fori(1, DEG) as t:
                    state_step(layer, t, False)
                h_start((layer + 1) * TILES - 1, NT - 1)
                h_split((layer + 1) * TILES - 1, NT - 1)

            table_rows(0)
            all_steps(0)
            table_rows(1)
            dve.wait_ge(xres_loaded, 16)
            nc.vector.tensor_tensor(x_res, x_res, bl2[:, None, :].to_broadcast([P, NBLK, C]), ALU.add
                                    ).then_inc(xres_ready, 1)
            all_steps(1)
            dve.wait_ge(xres_ready, 1)
            for k in range(NT):
                bs = slice(k * BPT, (k + 1) * BPT)
                dve.wait_ge(out_psum, k + 1)
                nc.vector.tensor_tensor(y[:, bs, :], ps[:, k, :].rearrange("p (b c) -> p b c", c=C),
                                        x_res[:, bs, :], ALU.add).then_inc(y_sum, 1)
                dve.wait_ge(y_sum, k + 1)
                for b in range(k * BPT, (k + 1) * BPT):
                    nc.vector.bn_stats(stats[:, b, :], y[:, b, :]).then_inc(stats_ready, 1)
            for b in range(NBLK):
                dve.wait_ge(stats_ready, b + 1)
                nc.vector.bn_aggr(mv[:, b, :], stats[:, b, :]).then_inc(mv_ready, 1)
            dve.wait_ge(std_ready, 1)
            nc.vector.reciprocal(rstd[:, :], rstd[:, :]).then_inc(rstd_ready, 1)
            dve.wait_ge(rstd_ready, 1)
            for b in range(NBLK):
                nc.vector.tensor_scalar(y[:, b, :], y[:, b, :], mv[:, b, 0:1], rstd[:, b:b + 1],
                                        ALU.subtract, ALU.mult).then_inc(y_ready, 1)


_WEIGHTS = ["wih", "whh", "bih", "bhh", "wl", "bl", "wr"]


def kernel(**inputs):
    import numpy as np
    import concourse.bacc as bacc
    from concourse import mybir as mb
    from concourse.bass_utils import run_bass_kernel_spmd

    nc = bacc.Bacc("TRN2", target_bir_lowering=False, num_devices=1)
    arrays = {}

    def given(name):
        a = np.ascontiguousarray(inputs[name])
        arrays[f"in_{name}"] = a
        return nc.dram_tensor(f"in_{name}", a.shape, mb.dt.from_np(a.dtype), kind="ExternalInput").ap()

    x, src = given("x"), given("src")
    layers = [[given(f"L0_gnn_conv{i}_{w}") for w in _WEIGHTS] for i in (1, 2)]
    shape = inputs["x"].shape
    table = [nc.dram_tensor(f"table{i}", (shape[0], 4 * shape[1]), mb.dt.float32, kind="Internal").ap()
             for i in (1, 2)]
    out = nc.dram_tensor("out", shape, mb.dt.float32, kind="ExternalOutput").ap()
    sage_lstm_resnorm_kernel(nc, x, src, layers, table, out)
    r = run_bass_kernel_spmd(nc, [arrays], core_ids=[0])
    return r.results[0]["out"]
```

```python
import concourse.bass as bass
from concourse import mybir
from contextlib import ExitStack


def sage_lstm_resnorm_kernel(nc, x, src, layers, table, out):
    fp32 = mybir.dt.float32
    fp16 = mybir.dt.float16
    i32 = mybir.dt.int32
    u32 = mybir.dt.uint32
    ALU = mybir.AluOpType
    ACT = mybir.ActivationFunctionType

    P = 128
    N, C = x.shape
    DEG = src.shape[0] // N
    NQ = 4
    GW = NQ * C
    TILE = 512
    BPT = TILE // P
    NBLK = N // P
    NT = N // TILE
    LAYERS = 2
    ROWSLOTS = 4
    W_SCALE = 2.0 ** 4
    H_SCALE = 2.0 ** 6
    Z_SCALE = W_SCALE * H_SCALE
    GATE = [1, 0, 3, 2]
    EPS = 1e-5
    W_GROUPS = 3
    TILES = DEG * NT

    ctx = ExitStack()
    with ctx:
        def sb(name, shape, dt=fp32):
            return ctx.enter_context(nc.sbuf_tensor(name, shape, dt))

        def sem(name):
            return ctx.enter_context(nc.semaphore(name))

        idx = sb("idx", [P, NBLK, DEG + 1], i32)
        stage = sb("stage", [P, NT, BPT], i32)
        ident = sb("ident", [P, P])
        x_in = sb("x_in", [P, NBLK, C])
        x_split = sb("x_split", [P, 2, N], fp16)
        h1_split = sb("h1_split", [P, 2, N], fp16)
        h1_tmp = sb("h1_tmp", [P, 2, TILE])
        h32 = sb("h32", [P, 2, TILE])
        h_hi = sb("h_hi", [P, N], fp16)
        h_lo = sb("h_lo", [P, N], fp16)
        rows = sb("rows", [P, ROWSLOTS, BPT, GW])
        cg = sb("cg", [P, NT + 2, TILE])
        sig = sb("sig", [P, 2, 3, TILE])
        prod = sb("prod", [P, 2, 2, TILE])
        tanc = sb("tanc", [P, 2, TILE])
        w_in = sb("w_in", [P, LAYERS, 2 * NQ + 2, C])
        b_in = sb("b_in", [P, LAYERS, 2, GW])
        b_sum = sb("b_sum", [P, LAYERS, GW])
        bias = sb("bias", [P, LAYERS, GW])
        w_hi = sb("w_hi", [P, LAYERS, W_GROUPS, GW], fp16)
        w_lo = sb("w_lo", [P, LAYERS, W_GROUPS, GW], fp16)
        bl1 = sb("bl1", [P, 1])
        bl2 = sb("bl2", [P, C])
        stats = sb("stats", [P, NBLK, 6])
        mv = sb("mv", [P, NBLK, 2])
        std = sb("std", [P, NBLK])
        rstd = sb("rstd", [P, NBLK])
        shift = sb("shift", [P, NBLK])
        epst = sb("epst", [P, 1])
        ps = ctx.enter_context(nc.psum_tensor("ps", [P, 8, TILE], fp32))

        y = x_in

        PARTS = ((w_hi, 0), (w_lo, 0), (w_hi, 1))

        x_loaded = [sem(f"x_loaded{k}") for k in range(NT)]
        idx_loaded = sem("idx_loaded")
        idx_wrapped = sem("idx_wrapped")
        first_loaded = sem("first_loaded")
        later_loaded = sem("later_loaded")
        ident_zero = sem("ident_zero")
        ident_ready = sem("ident_ready")
        w_transposed = sem("w_transposed")
        w_ready = sem("w_ready")
        w_hi_ready = sem("w_hi_ready")
        xT_psum = sem("xT_psum")
        x_hi_ready = sem("x_hi_ready")
        x_ready = sem("x_ready")
        table_psum = sem("table_psum")
        table_evac = sem("table_evac")
        table_stored = [sem(f"table_stored{k}") for k in range(ROWSLOTS)]
        staged = sem("staged")
        gathered = [sem(f"gathered{k}") for k in range(ROWSLOTS)]
        gather_turn = sem("gather_turn")
        rows_used = sem("rows_used")
        gates_ready = sem("gates_ready")
        acts_ready = sem("acts_ready")
        prod_ready = sem("prod_ready")
        c_ready = sem("c_ready")
        tanc_ready = sem("tanc_ready")
        h32_ready = sem("h32_ready")
        hi_ready = sem("hi_ready")
        h_ready = sem("h_ready")
        lin_ready = sem("lin_ready")
        h1_relu = sem("h1_relu")
        h1_hi = sem("h1_hi")
        h1_ready = sem("h1_ready")
        out_psum = sem("out_psum")
        y_sum = sem("y_sum")
        shift_ready = sem("shift_ready")
        b_summed = sem("b_summed")
        bias_ready = sem("bias_ready")
        xres_ready = sem("xres_ready")
        stats_ready = sem("stats_ready")
        mv_ready = sem("mv_ready")
        std_ready = sem("std_ready")
        rstd_ready = sem("rstd_ready")
        y_ready = sem("y_ready")
        stored = sem("stored")
        eps_ready = sem("eps_ready")

        block = ctx.enter_context(nc.Block())

        def blk(b):
            return slice(b * P, (b + 1) * P)

        def tl(j):
            return slice(j * TILE, (j + 1) * TILE)

        WIH, WHH, WLR = range(W_GROUPS)
        GROUPS = [(layer, g) for layer in range(LAYERS) for g in range(W_GROUPS)]
        FIRST_LOADS = 3
        LATER_LOADS = 6 * LAYERS + 2 - FIRST_LOADS

        @block.sync
        def _(sp):
            for k in range(NT):
                sp.dma_start(x_in[:, k * BPT:(k + 1) * BPT, :],
                             x[k * TILE:(k + 1) * TILE, :].rearrange("(b p) c -> p b c", p=P)
                             ).then_inc(x_loaded[k], 16)
                if k == 3:
                    sp.dma_start(idx[:, :, 0:DEG], src.rearrange("(b p t) -> p b t", p=P, t=DEG)
                                 ).then_inc(idx_loaded, 16)
            HALF = BPT // 2
            for layer in range(LAYERS):
                for m in range(NBLK // HALF):
                    n = layer * NT + m * HALF // BPT
                    b = m * HALF % BPT
                    sp.wait_ge(table_evac, layer * NBLK + (m + 1) * HALF)
                    sp.dma_start(table[layer][m * HALF * P:(m + 1) * HALF * P, :].rearrange("(b p) g -> p b g", p=P),
                                 rows[:, n % ROWSLOTS, b:b + HALF, :]).then_inc(table_stored[n % ROWSLOTS], 16)
            for k in range(NT):
                sp.wait_ge(y_ready, (k + 1) * BPT)
                sp.dma_start(out[k * TILE:(k + 1) * TILE, :].rearrange("(b p) c -> p b c", p=P),
                             y[:, k * BPT:(k + 1) * BPT, :]).then_inc(stored, 16)
            sp.wait_ge(stored, 16 * NT)

        @block.gpsimd
        def _(pool):
            nc.gpsimd.memset(ident[:, :], 0.0).then_inc(ident_zero, 1)
            pool.wait_ge(ident_zero, 1)
            nc.gpsimd.affine_select(out=ident[:, :], in_=ident[:, :], compare_op=ALU.not_equal, fill=1.0,
                                    base=0, pattern=[[-1, P]], channel_multiplier=1).then_inc(ident_ready, 1)

            def gather_step(layer, t, first):
                for j in range(NT):
                    tile = layer * TILES + t * NT + j
                    slot = j % ROWSLOTS
                    if not (first and layer == 0 and j < ROWSLOTS):
                        pool.wait_ge(rows_used, tile - ROWSLOTS + 1)
                    pool.wait_ge(staged, tile + 1)
                    pool.sem_inc(gather_turn, 1)
                    for b in range(BPT):
                        nc.gpsimd.indirect_dma_start(
                            rows[:, slot, b, :], None, table[layer],
                            bass.IndirectOffsetOnAxis(stage[:, j, b:b + 1].bitcast(u32), 0)
                        ).then_inc(gathered[slot], 16)

            for layer in range(LAYERS):
                for k in range(ROWSLOTS):
                    pool.wait_ge(table_stored[k], 2 * 16 * (layer + 1) * NT // ROWSLOTS)
                gather_step(layer, 0, True)
                with pool.Fori(1, DEG) as t:
                    gather_step(layer, t, False)
            pool.wait_ge(later_loaded, 16 * LATER_LOADS)
            pool.wait_ge(xT_psum, NT)
            for k in range(NT):
                bs = slice(k * BPT, (k + 1) * BPT)
                nc.gpsimd.tensor_tensor(x_in[:, bs, :], x_in[:, bs, :], bl2[:, None, :].to_broadcast([P, BPT, C]),
                                        ALU.add).then_inc(xres_ready, 1)

        @block.tensor
        def _(pe):
            def transpose_weights(n):
                layer, group = GROUPS[n]
                if n >= 2:
                    pe.wait_ge(w_ready, n - 1)
                cols = [2 * NQ, 2 * NQ + 1] if group == WLR else [group * NQ + q for q in GATE]
                for k, w in enumerate(cols):
                    last = nc.tensor.transpose(ps[:, n % 2, blk(k)], w_in[:, layer, w, :], ident[:, :])
                last.then_inc(w_transposed, 1)

            def transpose_x(k):
                pe.wait_ge(x_loaded[k], 16)
                if k >= 2:
                    pe.wait_ge(x_ready, k - 1)
                for b in range(BPT):
                    last = nc.tensor.transpose(ps[:, 2 + k % 2, blk(b)], x_in[:, k * BPT + b, :], ident[:, :])
                last.then_inc(xT_psum, 1)

            def table_rows(layer, k, v, bank):
                for b in range(k * BPT, (k + 1) * BPT):
                    n = layer * NBLK + b
                    if b >= 4:
                        pe.wait_ge(table_evac, n - 3)
                    for m, (w, part) in enumerate(PARTS):
                        last = nc.tensor.matmul(ps[:, bank + n % 4, :], v[:, part, blk(b)], w[:, layer, WIH, :],
                                                start=m == 0, stop=m == 2)
                    last.then_inc(table_psum, 1)

            def gates_step(layer, t, first):
                for j in range(NT):
                    tile = layer * TILES + t * NT + j
                    bank = j % 2 * NQ
                    slot = j % ROWSLOTS
                    pe.wait_ge(gathered[slot], (16 * BPT) * (layer * TILES // ROWSLOTS + t * (NT // ROWSLOTS)
                                                            + j // ROWSLOTS + 1))
                    if not (first and layer == 0 and j < 2):
                        pe.wait_ge(acts_ready, tile - 1)
                    for q in range(NQ):
                        for b in range(BPT):
                            last = nc.tensor.matmul(ps[:, bank + q, blk(b)], rows[:, slot, b, blk(q)], ident[:, :],
                                                    start=b == 0, stop=first and b == BPT - 1,
                                                    is_transpose=True, skip_group_check=True)
                    last.then_inc(rows_used, 1)
                    if first:
                        continue
                    pe.wait_ge(h_ready, tile - NT + 1)
                    for q in range(NQ):
                        for m, (w, part) in enumerate(PARTS):
                            last = nc.tensor.matmul(ps[:, bank + q, :], w[:, layer, WHH, blk(q)],
                                                    (h_hi, h_lo)[part][:, tl(j)],
                                                    start=False, stop=m == 2, skip_group_check=True)
                    last.then_inc(gates_ready, 1)

            def all_steps(layer):
                gates_step(layer, 0, True)
                with pe.Fori(1, DEG) as t:
                    gates_step(layer, t, False)

            pe.wait_ge(ident_ready, 1)
            pe.wait_ge(first_loaded, 16 * FIRST_LOADS)
            transpose_weights(0)
            transpose_x(0)
            transpose_x(1)
            pe.wait_ge(w_ready, 1)
            for k in range(NT):
                pe.wait_ge(x_ready, k + 1)
                table_rows(0, k, x_split, 4)
                if k + 2 < NT:
                    transpose_x(k + 2)
            pe.wait_ge(later_loaded, 16 * LATER_LOADS)
            for n in range(1, len(GROUPS)):
                transpose_weights(n)
            pe.wait_ge(w_ready, len(GROUPS))
            pe.wait_ge(table_evac, NBLK)
            all_steps(0)
            for j in range(NT):
                pe.wait_ge(acts_ready, TILES if j >= 4 else TILES - 1)
                for m, (w, part) in enumerate(PARTS):
                    nc.tensor.matmul(ps[:, j, :], w[:, 0, WLR, C:2 * C], x_split[:, part, tl(j)],
                                     start=m == 0, stop=False)
                pe.wait_ge(h_ready, TILES - NT + j + 1)
                for m, (w, part) in enumerate(PARTS):
                    last = nc.tensor.matmul(ps[:, j, :], w[:, 0, WLR, 0:C], (h_hi, h_lo)[part][:, tl(j)],
                                            start=False, stop=m == 2)
                last.then_inc(lin_ready, 1)
            pe.wait_ge(h1_relu, 4)
            for k in range(NT):
                pe.wait_ge(h1_ready, k + 1)
                table_rows(1, k, h1_split, 0)
            pe.wait_ge(table_evac, 2 * NBLK)
            pe.wait_ge(h1_relu, NT)
            all_steps(1)
            for k in range(NT):
                pe.wait_ge(acts_ready, 2 * TILES if k >= 4 else 2 * TILES - 1)
                pe.wait_ge(h_ready, 2 * TILES - NT + k + 1)
                for b in range(BPT):
                    n = k * BPT + b
                    for m, (w, part) in enumerate(PARTS):
                        nc.tensor.matmul(ps[:, k, blk(b)], h1_split[:, part, blk(n)], w[:, 1, WLR, C:2 * C],
                                         start=m == 0, stop=False, skip_group_check=True)
                    for m, (w, part) in enumerate(PARTS):
                        last = nc.tensor.matmul(ps[:, k, blk(b)], (h_hi, h_lo)[part][:, blk(n)],
                                                w[:, 1, WLR, 0:C],
                                                start=False, stop=m == 2, skip_group_check=True)
                last.then_inc(out_psum, 1)

        @block.scalar
        def _(act):
            wih, whh, bih, bhh, wl, bl, wr = range(7)

            def load_w(layer, at, n, w, done):
                act.dma_start(w_in[:, layer, at:at + n, :], layers[layer][w].rearrange("(q p) c -> p q c", p=P)
                              ).then_inc(done, 16)

            def load_b(layer, done):
                for k, v in enumerate((bih, bhh)):
                    act.dma_start(b_in[:, layer, k, :],
                                  layers[layer][v].rearrange("(o g) -> o g", o=1).to_broadcast([P, GW])
                                  ).then_inc(done, 16)

            load_w(0, 0, NQ, wih, first_loaded)
            load_b(0, first_loaded)
            load_w(0, NQ, NQ, whh, later_loaded)
            for layer in range(LAYERS):
                load_w(layer, 2 * NQ, 1, wl, later_loaded)
                load_w(layer, 2 * NQ + 1, 1, wr, later_loaded)
            load_w(1, 0, NQ, wih, later_loaded)
            load_w(1, NQ, NQ, whh, later_loaded)
            load_b(1, later_loaded)
            act.dma_start(bl1[:, :], layers[0][bl].rearrange("(c o) -> c o", o=1)).then_inc(later_loaded, 16)
            act.dma_start(bl2[:, :], layers[1][bl].rearrange("(o c) -> o c", o=1).to_broadcast([P, C])
                          ).then_inc(later_loaded, 16)
            for k in range(NT):
                act.wait_ge(xT_psum, k + 1)
                nc.scalar.copy(x_split[:, 0, tl(k)], ps[:, 2 + k % 2, :]).then_inc(x_hi_ready, 1)

            def tanh_c(tile, j):
                act.wait_ge(c_ready, tile + 1)
                nc.scalar.activation(tanc[:, j % 2, :], cg[:, j, :], ACT.Tanh).then_inc(tanc_ready, 1)

            def act_step(layer, t, first):
                for j in range(NT):
                    tile = layer * TILES + t * NT + j
                    bank = j % 2 * NQ
                    if first:
                        act.wait_ge(rows_used, tile + 1)
                    else:
                        act.wait_ge(gates_ready, tile + 1 - NT * (layer + 1))
                    if not (first and layer == 0 and j < 2):
                        act.wait_ge(h32_ready, tile - 1)
                    nc.scalar.activation(sig[:, j % 2, :, :], ps[:, bank:bank + 3, :], ACT.Sigmoid,
                                         scale=1.0 / Z_SCALE)
                    nc.scalar.activation(cg[:, NT + j % 2, :], ps[:, bank + 3, :], ACT.Tanh,
                                         scale=1.0 / Z_SCALE).then_inc(acts_ready, 1)
                    if not (first and j == 0):
                        tanh_c(tile - 1, (j - 1) % NT)

            def all_steps(layer):
                act_step(layer, 0, True)
                with act.Fori(1, DEG) as t:
                    act_step(layer, t, False)
                tanh_c((layer + 1) * TILES - 1, NT - 1)

            all_steps(0)
            for j in range(NT):
                act.wait_ge(lin_ready, j + 1)
                if j >= 2:
                    act.wait_ge(h1_ready, j - 1)
                nc.scalar.activation(h1_tmp[:, j % 2, :], ps[:, j, :], ACT.Relu, bias=bl1[:, :],
                                     scale=1.0 / Z_SCALE).then_inc(h1_relu, 1)
                act.wait_ge(h1_relu, j + 1)
                nc.scalar.copy(h1_split[:, 0, tl(j)], h1_tmp[:, j % 2, :]).then_inc(h1_hi, 1)
            all_steps(1)
            def normalise(k):
                act.wait_ge(shift_ready, k + 1)
                for b in range(k * BPT, (k + 1) * BPT):
                    nc.scalar.activation(y[:, b, :], y[:, b, :], ACT.Identity, bias=shift[:, b:b + 1],
                                         scale=rstd[:, b:b + 1]).then_inc(y_ready, 1)

            for k in range(NT):
                bs = slice(k * BPT, (k + 1) * BPT)
                act.wait_ge(mv_ready, (k + 1) * BPT)
                nc.scalar.activation(std[:, bs], mv[:, bs, 1], ACT.Sqrt, bias=epst[:, :]).then_inc(std_ready, 1)
                if k > 0:
                    normalise(k - 1)
            normalise(NT - 1)

        @block.vector
        def _(dve):
            nc.vector.memset(epst[:, :], EPS).then_inc(eps_ready, 1)

            def make_bias(layer):
                for k, q in enumerate(GATE):
                    nc.vector.tensor_tensor(b_sum[:, layer, blk(k)], b_in[:, layer, 0, blk(q)],
                                            b_in[:, layer, 1, blk(q)], ALU.add).then_inc(b_summed, 1)
                dve.wait_ge(b_summed, (layer + 1) * NQ)
                nc.vector.tensor_scalar(bias[:, layer, :], b_sum[:, layer, :], Z_SCALE, None, ALU.mult
                                        ).then_inc(bias_ready, 1)

            def split_weights(n):
                layer, group = GROUPS[n]
                dve.wait_ge(w_transposed, n + 1)
                if group == WLR:
                    pieces = [(slice(0, C), W_SCALE), (slice(C, 2 * C), Z_SCALE)]
                else:
                    pieces = [(slice(0, GW), Z_SCALE if group == WIH else W_SCALE)]
                for cols, scale in pieces:
                    last = nc.vector.tensor_scalar(w_hi[:, layer, group, cols], ps[:, n % 2, cols], scale, None,
                                                   ALU.mult)
                last.then_inc(w_hi_ready, 1)
                dve.wait_ge(w_hi_ready, n + 1)
                for cols, scale in pieces:
                    last = nc.vector.scalar_tensor_tensor(w_lo[:, layer, group, cols], ps[:, n % 2, cols], scale,
                                                          w_hi[:, layer, group, cols], ALU.mult, ALU.subtract)
                last.then_inc(w_ready, 1)

            def x_low(k):
                dve.wait_ge(x_hi_ready, k + 1)
                nc.vector.tensor_tensor(x_split[:, 1, tl(k)], ps[:, 2 + k % 2, :], x_split[:, 0, tl(k)],
                                        ALU.subtract).then_inc(x_ready, 1)

            def table_rows(layer, k, bank):
                n = layer * NT + k
                if n >= ROWSLOTS:
                    dve.wait_ge(table_stored[n % ROWSLOTS], 2 * 16 * (n // ROWSLOTS))
                for b in range(n * BPT, (n + 1) * BPT):
                    dve.wait_ge(table_psum, b + 1)
                    nc.vector.tensor_tensor(rows[:, n % ROWSLOTS, b % BPT, :], ps[:, bank + b % 4, :],
                                            bias[:, layer, :], ALU.add).then_inc(table_evac, 1)

            def h_start(tile, j):
                dve.wait_ge(tanc_ready, tile + 1)
                nc.vector.scalar_tensor_tensor(h32[:, j % 2, :], sig[:, j % 2, 2, :], H_SCALE, tanc[:, j % 2, :],
                                               ALU.mult, ALU.mult).then_inc(h32_ready, 1)

            def h_split(tile, j):
                dve.wait_ge(h32_ready, tile + 1)
                nc.vector.tensor_copy(h_hi[:, tl(j)], h32[:, j % 2, :]).then_inc(hi_ready, 1)
                dve.wait_ge(hi_ready, tile + 1)
                nc.vector.tensor_tensor(h_lo[:, tl(j)], h32[:, j % 2, :], h_hi[:, tl(j)], ALU.subtract
                                        ).then_inc(h_ready, 1)

            def state_step(layer, t, first):
                for j in range(NT):
                    tile = layer * TILES + t * NT + j
                    g = NT + j % 2
                    dve.wait_ge(acts_ready, tile + 1)
                    if first:
                        nc.vector.tensor_tensor(cg[:, j, :], sig[:, j % 2, 1, :], cg[:, g, :], ALU.mult
                                                ).then_inc(c_ready, 1)
                        if j > 0:
                            h_start(tile - 1, j - 1)
                    else:
                        nc.vector.tensor_tensor(prod[:, j % 2, :, :], sig[:, j % 2, 0:2, :],
                                                cg[:, j:g + 1:g - j, :], ALU.mult).then_inc(prod_ready, 1)
                        h_start(tile - 1, (j - 1) % NT)
                        dve.wait_ge(prod_ready, tile + 1 - NT * (layer + 1))
                        nc.vector.tensor_tensor(cg[:, j, :], prod[:, j % 2, 0, :], prod[:, j % 2, 1, :], ALU.add
                                                ).then_inc(c_ready, 1)
                    nc.vector.tensor_copy(stage[:, j, :], idx[:, j * BPT:(j + 1) * BPT, t + 1]).then_inc(staged, 1)
                    if not (first and j == 0):
                        h_split(tile - 1, (j - 1) % NT)

            def all_steps(layer):
                state_step(layer, 0, True)
                with dve.Fori(1, DEG) as t:
                    state_step(layer, t, False)
                h_start((layer + 1) * TILES - 1, NT - 1)
                h_split((layer + 1) * TILES - 1, NT - 1)

            dve.wait_ge(first_loaded, 16 * FIRST_LOADS)
            split_weights(0)
            make_bias(0)
            dve.wait_ge(bias_ready, 1)
            x_low(0)
            x_low(1)
            for k in range(NT):
                table_rows(0, k, 4)
                if k + 2 < NT:
                    x_low(k + 2)
                if k == 4:
                    dve.wait_ge(idx_loaded, 16)
                    nc.vector.tensor_copy(stage[:, :, :].rearrange("p j b -> p (j b)"), idx[:, :, 0]
                                          ).then_inc(staged, NT)
                    nc.vector.tensor_copy(idx[:, :, DEG], idx[:, :, 0]).then_inc(idx_wrapped, 1)
            for n in range(1, len(GROUPS)):
                split_weights(n)
            dve.wait_ge(later_loaded, 16 * LATER_LOADS)
            make_bias(1)
            dve.wait_ge(bias_ready, 2)
            dve.wait_ge(idx_wrapped, 1)
            all_steps(0)
            for j in range(NT):
                dve.wait_ge(h1_hi, j + 1)
                nc.vector.tensor_tensor(h1_split[:, 1, tl(j)], h1_tmp[:, j % 2, :], h1_split[:, 0, tl(j)],
                                        ALU.subtract).then_inc(h1_ready, 1)
            for k in range(NT):
                table_rows(1, k, 0)
            all_steps(1)

            def scales(k):
                bs = slice(k * BPT, (k + 1) * BPT)
                dve.wait_ge(std_ready, k + 1)
                nc.vector.reciprocal(rstd[:, bs], std[:, bs]).then_inc(rstd_ready, 1)
                dve.wait_ge(rstd_ready, k + 1)
                nc.vector.scalar_tensor_tensor(shift[:, bs], mv[:, bs, 0], -1.0, rstd[:, bs], ALU.mult, ALU.mult
                                               ).then_inc(shift_ready, 1)

            for k in range(NT):
                bs = slice(k * BPT, (k + 1) * BPT)
                dve.wait_ge(out_psum, k + 1)
                dve.wait_ge(xres_ready, k + 1)
                nc.vector.scalar_tensor_tensor(y[:, bs, :], ps[:, k, :].rearrange("p (b c) -> p b c", c=C),
                                               1.0 / Z_SCALE, x_in[:, bs, :], ALU.mult, ALU.add).then_inc(y_sum, 1)
                dve.wait_ge(y_sum, k + 1)
                for b in range(k * BPT, (k + 1) * BPT):
                    nc.vector.bn_stats(stats[:, b, :], y[:, b, :]).then_inc(stats_ready, 1)
                if k > 0:
                    scales(k - 1)
                for b in range(k * BPT, (k + 1) * BPT):
                    dve.wait_ge(stats_ready, b + 1)
                    nc.vector.bn_aggr(mv[:, b, :], stats[:, b, :]).then_inc(mv_ready, 1)
            scales(NT - 1)


_WEIGHTS = ["wih", "whh", "bih", "bhh", "wl", "bl", "wr"]


def kernel(**inputs):
    import numpy as np
    import concourse.bacc as bacc
    from concourse import mybir as mb
    from concourse.bass_utils import run_bass_kernel_spmd

    nc = bacc.Bacc("TRN2", target_bir_lowering=False, num_devices=1)
    arrays = {}

    def given(name):
        a = np.ascontiguousarray(inputs[name])
        arrays[f"in_{name}"] = a
        return nc.dram_tensor(f"in_{name}", a.shape, mb.dt.from_np(a.dtype), kind="ExternalInput").ap()

    x, src = given("x"), given("src")
    layers = [[given(f"L0_gnn_conv{i}_{w}") for w in _WEIGHTS] for i in (1, 2)]
    shape = inputs["x"].shape
    table = [nc.dram_tensor(f"table{i}", (shape[0], 4 * shape[1]), mb.dt.float32, kind="Internal").ap()
             for i in (1, 2)]
    out = nc.dram_tensor("out", shape, mb.dt.float32, kind="ExternalOutput").ap()
    sage_lstm_resnorm_kernel(nc, x, src, layers, table, out)
    r = run_bass_kernel_spmd(nc, [arrays], core_ids=[0])
    return r.results[0]["out"]
```

```python
import concourse.bass as bass
from concourse import mybir
from contextlib import ExitStack


def sage_lstm_resnorm_kernel(nc, x, src, layers, table, h1_rows, out):
    fp32 = mybir.dt.float32
    fp16 = mybir.dt.float16
    i32 = mybir.dt.int32
    u32 = mybir.dt.uint32
    ALU = mybir.AluOpType
    ACT = mybir.ActivationFunctionType

    P = 128
    N, C = x.shape
    DEG = src.shape[0] // N
    NQ = 4
    GW = NQ * C
    TILE = 512
    BPT = TILE // P
    NBLK = N // P
    NT = N // TILE
    LAYERS = 2
    ROWSLOTS = 4
    H1SLOTS = 4
    SIGSLOTS = 4
    W_SCALE = 2.0 ** 4
    H_SCALE = 2.0 ** 6
    Z_SCALE = W_SCALE * H_SCALE
    GATE = [1, 0, 3, 2]
    EPS = 1e-5
    W_GROUPS = 3
    TILES = DEG * NT

    ctx = ExitStack()
    with ctx:
        def sb(name, shape, dt=fp32):
            return ctx.enter_context(nc.sbuf_tensor(name, shape, dt))

        def sem(name):
            return ctx.enter_context(nc.semaphore(name))

        idx = sb("idx", [P, NBLK, DEG + 1], i32)
        stage = sb("stage", [P, NT, BPT], i32)
        ident = sb("ident", [P, P])
        x_in = sb("x_in", [P, NBLK, C])
        x_split = sb("x_split", [P, 2, N], fp16)
        h1_split = sb("h1_split", [P, 2, N], fp16)
        h1_tmp = sb("h1_tmp", [P, 2, TILE])
        h32 = sb("h32", [P, 2, TILE])
        h_hi = sb("h_hi", [P, N], fp16)
        h_lo = sb("h_lo", [P, N], fp16)
        rows = sb("rows", [P, ROWSLOTS, BPT, GW])
        cg = sb("cg", [P, NT + 2, TILE])
        sig = sb("sig", [P, SIGSLOTS, 3, TILE])
        prod = sb("prod", [P, 2, 2, TILE])
        tanc = sb("tanc", [P, 2, TILE])
        w_in = sb("w_in", [P, LAYERS, 2 * NQ + 2, C])
        b_in = sb("b_in", [P, LAYERS, 2, GW])
        bT_in = sb("bT_in", [P, LAYERS, 2, NQ])
        biasT = sb("biasT", [P, LAYERS, NQ])
        b_sum = sb("b_sum", [P, LAYERS, GW])
        bias = sb("bias", [P, LAYERS, GW])
        w_hi = sb("w_hi", [P, LAYERS, W_GROUPS, GW], fp16)
        w_lo = sb("w_lo", [P, LAYERS, W_GROUPS, GW], fp16)
        bl1 = sb("bl1", [P, 1])
        bl2 = sb("bl2", [P, C])
        stats = sb("stats", [P, NBLK, 6])
        mv = sb("mv", [P, NBLK, 2])
        std = sb("std", [P, NBLK])
        rstd = sb("rstd", [P, NBLK])
        shift = sb("shift", [P, NBLK])
        epst = sb("epst", [P, 1])
        ps = ctx.enter_context(nc.psum_tensor("ps", [P, 8, TILE], fp32))

        y = x_in
        in_rows = cg[:, 0:NT, :].rearrange("p j (b c) -> p j b c", c=C)
        h1_out = prod[:, :, :, :].rearrange("p a b n -> p (a b) n")

        PARTS = ((w_hi, 0), (w_lo, 0), (w_hi, 1))

        x_loaded = [sem(f"x_loaded{k}") for k in range(NT)]
        idx0_loaded = sem("idx0_loaded")
        idx_loaded = sem("idx_loaded")
        idx_wrapped = sem("idx_wrapped")
        wih_loaded = sem("wih_loaded")
        first_b_loaded = sem("first_b_loaded")
        later_loaded = sem("later_loaded")
        ident_zero = sem("ident_zero")
        ident_ready = sem("ident_ready")
        w_transposed = sem("w_transposed")
        w_ready = sem("w_ready")
        w_hi_ready = sem("w_hi_ready")
        xT_psum = sem("xT_psum")
        x_hi_ready = sem("x_hi_ready")
        x_ready = sem("x_ready")
        table_psum = sem("table_psum")
        table_evac = sem("table_evac")
        table_stored = [sem(f"table_stored{k}") for k in range(ROWSLOTS)]
        staged = sem("staged")
        gathered = [sem(f"gathered{k}") for k in range(ROWSLOTS)]
        gather_turn = sem("gather_turn")
        rows_free = sem("rows_free")
        in_gathered = [sem(f"in_gathered{k}") for k in range(NT)]
        inT_psum = sem("inT_psum")
        in_hi = sem("in_hi")
        first_gate_read = sem("first_gate_read")
        in_split = sem("in_split")
        h1_rows_psum = sem("h1_rows_psum")
        h1_rows_ready = sem("h1_rows_ready")
        h1_stored = [sem(f"h1_stored{k}") for k in range(H1SLOTS)]
        biasT_ready = sem("biasT_ready")
        gates_ready = sem("gates_ready")
        acts_ready = sem("acts_ready")
        prod_ready = sem("prod_ready")
        c_ready = sem("c_ready")
        tanc_ready = sem("tanc_ready")
        h32_ready = sem("h32_ready")
        hi_ready = sem("hi_ready")
        h_ready = sem("h_ready")
        lin_ready = sem("lin_ready")
        h1_relu = sem("h1_relu")
        h1_hi = sem("h1_hi")
        h1_ready = sem("h1_ready")
        out_psum = sem("out_psum")
        y_sum = sem("y_sum")
        shift_ready = sem("shift_ready")
        b_summed = sem("b_summed")
        bias_ready = sem("bias_ready")
        xres_ready = sem("xres_ready")
        stats_ready = sem("stats_ready")
        mv_ready = sem("mv_ready")
        std_ready = sem("std_ready")
        rstd_ready = sem("rstd_ready")
        y_ready = sem("y_ready")
        stored = sem("stored")
        eps_ready = sem("eps_ready")

        block = ctx.enter_context(nc.Block())

        def blk(b):
            return slice(b * P, (b + 1) * P)

        def tl(j):
            return slice(j * TILE, (j + 1) * TILE)

        WIH, WHH, WLR = range(W_GROUPS)
        GROUPS = [(layer, g) for layer in range(LAYERS) for g in range(W_GROUPS)]
        LATER_LOADS = 8 * LAYERS + 2 - 3
        FIRST_ORDER = [[("T", j) for j in range(NT)] + [("M", j) for j in range(NT)],
                       [("T", 0), ("T", 1)] + [p for j in range(NT - 2) for p in (("M", j), ("T", j + 2))]
                       + [("M", NT - 2), ("M", NT - 1)]]
        T_BANK = [[j for j in range(NT)], [j % 2 * NQ for j in range(NT)]]
        LOOPED = TILES - NT

        wih, whh, bih, bhh, wl, bl, wr = range(7)

        def load_w(eng, layer, at, n, w, done):
            eng.dma_start(w_in[:, layer, at:at + n, :], layers[layer][w].rearrange("(q p) c -> p q c", p=P)
                          ).then_inc(done, 16)

        def load_b(eng, layer, done):
            for k, v in enumerate((bih, bhh)):
                eng.dma_start(b_in[:, layer, k, :],
                              layers[layer][v].rearrange("(o g) -> o g", o=1).to_broadcast([P, GW])
                              ).then_inc(done, 16)

        def w_pieces(group):
            if group == WLR:
                return [(slice(0, C), W_SCALE), (slice(C, 2 * C), Z_SCALE)]
            return [(slice(0, GW), Z_SCALE if group == WIH else W_SCALE)]

        @block.sync
        def _(sp):
            idx_dram = src.rearrange("(b p t) -> p b t", p=P, t=DEG)
            sp.dma_start(idx[:, 0:BPT, 0:DEG], idx_dram[:, 0:BPT, :]).then_inc(idx0_loaded, 16)
            for k in range(NT):
                sp.dma_start(x_in[:, k * BPT:(k + 1) * BPT, :],
                             x[k * TILE:(k + 1) * TILE, :].rearrange("(b p) c -> p b c", p=P)
                             ).then_inc(x_loaded[k], 16)
                if k == 1:
                    sp.dma_start(idx[:, BPT:, 0:DEG], idx_dram[:, BPT:, :]).then_inc(idx_loaded, 16)
            load_w(sp, 0, NQ, NQ, whh, later_loaded)
            for layer in range(LAYERS):
                load_w(sp, layer, 2 * NQ, 1, wl, later_loaded)
                load_w(sp, layer, 2 * NQ + 1, 1, wr, later_loaded)
            load_w(sp, 1, 0, NQ, wih, later_loaded)
            load_w(sp, 1, NQ, NQ, whh, later_loaded)
            load_b(sp, 1, later_loaded)
            for layer in range(LAYERS):
                for k, v in enumerate((bih, bhh)):
                    with nc.allow_non_contiguous_dma("the biases with the features on the partitions, 2 KB each"):
                        sp.dma_start(bT_in[:, layer, k, :], layers[layer][v].rearrange("(q p) -> p q", p=P)
                                     ).then_inc(later_loaded, 16)
            sp.dma_start(bl1[:, :], layers[0][bl].rearrange("(c o) -> c o", o=1)).then_inc(later_loaded, 16)
            sp.dma_start(bl2[:, :], layers[1][bl].rearrange("(o c) -> o c", o=1).to_broadcast([P, C])
                         ).then_inc(later_loaded, 16)
            HALF = BPT // 2
            for layer in range(LAYERS):
                if layer == 1:
                    for k in range(NT):
                        sp.wait_ge(h1_rows_ready, k + 1)
                        sp.dma_start(h1_rows[k * TILE:(k + 1) * TILE, :].rearrange("(b p) c -> p b c", p=P),
                                     h1_out[:, k % H1SLOTS, :].rearrange("p (b c) -> p b c", c=C)
                                     ).then_inc(h1_stored[k % H1SLOTS], 16)
                for m in range(NBLK // HALF):
                    n = layer * NT + m * HALF // BPT
                    b = m * HALF % BPT
                    sp.wait_ge(table_evac, layer * NBLK + (m + 1) * HALF)
                    sp.dma_start(table[layer][m * HALF * P:(m + 1) * HALF * P, :].rearrange("(b p) g -> p b g", p=P),
                                 rows[:, n % ROWSLOTS, b:b + HALF, :]).then_inc(table_stored[n % ROWSLOTS], 16)
            for k in range(NT):
                sp.wait_ge(y_ready, (k + 1) * BPT)
                sp.dma_start(out[k * TILE:(k + 1) * TILE, :].rearrange("(b p) c -> p b c", p=P),
                             y[:, k * BPT:(k + 1) * BPT, :]).then_inc(stored, 16)
            sp.wait_ge(stored, 16 * NT)

        @block.gpsimd
        def _(pool):
            nc.gpsimd.memset(ident[:, :], 0.0).then_inc(ident_zero, 1)
            pool.wait_ge(ident_zero, 1)
            nc.gpsimd.affine_select(out=ident[:, :], in_=ident[:, :], compare_op=ALU.not_equal, fill=1.0,
                                    base=0, pattern=[[-1, P]], channel_multiplier=1).then_inc(ident_ready, 1)

            def gather_inputs(layer, source):
                for j in range(NT):
                    if layer == 0 and j == 1:
                        pool.wait_ge(idx_loaded, 16)
                    for b in range(BPT):
                        n = j * BPT + b
                        nc.gpsimd.indirect_dma_start(
                            in_rows[:, j, b, :], None, source,
                            bass.IndirectOffsetOnAxis(idx[:, n, 0:1].bitcast(u32), 0)
                        ).then_inc(in_gathered[j], 16)

            def gather_step(layer, t):
                for j in range(NT):
                    tile = layer * LOOPED + (t - 1) * NT + j
                    slot = j % ROWSLOTS
                    pool.wait_ge(rows_free, tile + 1)
                    pool.wait_ge(staged, tile + 1)
                    pool.sem_inc(gather_turn, 1)
                    for b in range(BPT):
                        nc.gpsimd.indirect_dma_start(
                            rows[:, slot, b, :], None, table[layer],
                            bass.IndirectOffsetOnAxis(stage[:, j, b:b + 1].bitcast(u32), 0)
                        ).then_inc(gathered[slot], 16)

            pool.sem_inc(rows_free, ROWSLOTS)
            pool.wait_ge(idx0_loaded, 16)
            for layer in range(LAYERS):
                if layer == 1:
                    for k in range(H1SLOTS):
                        pool.wait_ge(h1_stored[k], 16 * NT // H1SLOTS)
                gather_inputs(layer, (x, h1_rows)[layer])
                for k in range(ROWSLOTS):
                    pool.wait_ge(table_stored[k], 2 * 16 * (layer + 1) * NT // ROWSLOTS)
                with pool.Fori(1, DEG) as t:
                    gather_step(layer, t)
            pool.wait_ge(later_loaded, 16 * LATER_LOADS)
            pool.wait_ge(xT_psum, NT)
            for k in range(NT):
                bs = slice(k * BPT, (k + 1) * BPT)
                nc.gpsimd.tensor_tensor(x_in[:, bs, :], x_in[:, bs, :], bl2[:, None, :].to_broadcast([P, BPT, C]),
                                        ALU.add).then_inc(xres_ready, 1)

        @block.tensor
        def _(pe):
            def transpose_weights(n):
                layer, group = GROUPS[n]
                if n >= 4:
                    pe.wait_ge(w_ready, n - 3)
                cols = [2 * NQ, 2 * NQ + 1] if group == WLR else [group * NQ + q for q in GATE]
                for k, w in enumerate(cols):
                    last = nc.tensor.transpose(ps[:, n % 4, blk(k)], w_in[:, layer, w, :], ident[:, :])
                last.then_inc(w_transposed, 1)

            def transpose_x(k):
                pe.wait_ge(x_loaded[k], 16)
                if k >= 2:
                    pe.wait_ge(x_ready, k - 1)
                for b in range(BPT):
                    last = nc.tensor.transpose(ps[:, 2 + k % 2, blk(b)], x_in[:, k * BPT + b, :], ident[:, :])
                last.then_inc(xT_psum, 1)

            def table_rows(layer, k, v, bank):
                for b in range(k * BPT, (k + 1) * BPT):
                    n = layer * NBLK + b
                    if b >= 4:
                        pe.wait_ge(table_evac, n - 3)
                    for m, (w, part) in enumerate(PARTS):
                        last = nc.tensor.matmul(ps[:, bank + n % 4, :], v[:, part, blk(b)], w[:, layer, WIH, :],
                                                start=m == 0, stop=m == 2)
                    last.then_inc(table_psum, 1)

            def gates(layer, group, j, bank, start):
                for q in range(NQ):
                    for m, (w, part) in enumerate(PARTS):
                        last = nc.tensor.matmul(ps[:, bank + q, :], w[:, layer, group, blk(q)],
                                                (h_hi, h_lo)[part][:, tl(j)],
                                                start=start and m == 0, stop=m == 2, skip_group_check=True)
                last.then_inc(gates_ready, 1)

            def first_step(layer):
                for what, j in FIRST_ORDER[layer]:
                    if what == "T":
                        pe.wait_ge(in_gathered[j], 16 * BPT * (layer + 1))
                        if layer == 1 and j >= 2:
                            pe.wait_ge(first_gate_read, layer * NT + j - 1)
                        for b in range(BPT):
                            last = nc.tensor.transpose(ps[:, T_BANK[layer][j], blk(b)], in_rows[:, j, b, :],
                                                       ident[:, :])
                        last.then_inc(inT_psum, 1)
                        continue
                    pe.wait_ge(in_split, layer * NT + (j + 1 if layer == 1 or j >= 2 else (j + 1) * NQ))
                    if j >= 2:
                        pe.wait_ge(acts_ready, layer * TILES + j - 1)
                    gates(layer, WIH, j, j % 2 * NQ, True)

            def gates_step(layer, t):
                for j in range(NT):
                    tile = layer * TILES + t * NT + j
                    bank = j % 2 * NQ
                    slot = j % ROWSLOTS
                    pe.wait_ge(gathered[slot], (16 * BPT) * (layer * LOOPED // ROWSLOTS
                                                            + (t - 1) * (NT // ROWSLOTS) + j // ROWSLOTS + 1))
                    pe.wait_ge(acts_ready, tile - 1)
                    for q in range(NQ):
                        for b in range(BPT):
                            last = nc.tensor.matmul(ps[:, bank + q, blk(b)], rows[:, slot, b, blk(q)], ident[:, :],
                                                    start=b == 0, stop=False,
                                                    is_transpose=True, skip_group_check=True)
                    last.then_inc(rows_free, 1)
                    pe.wait_ge(h_ready, tile - NT + 1)
                    gates(layer, WHH, j, bank, False)

            def all_steps(layer):
                first_step(layer)
                with pe.Fori(1, DEG) as t:
                    gates_step(layer, t)

            def h1_by_rows(j):
                pe.wait_ge(h1_relu, j + 1)
                for b in range(BPT):
                    last = nc.tensor.transpose(ps[:, j, blk(b)], h1_tmp[:, j % 2, blk(b)], ident[:, :])
                last.then_inc(h1_rows_psum, 1)

            pe.wait_ge(ident_ready, 1)
            pe.wait_ge(wih_loaded, 16)
            transpose_weights(0)
            transpose_x(0)
            transpose_x(1)
            pe.wait_ge(w_ready, 1)
            for k in range(NT):
                pe.wait_ge(x_ready, k + 1)
                table_rows(0, k, x_split, 4)
                if k + 2 < NT:
                    transpose_x(k + 2)
            pe.wait_ge(later_loaded, 16 * LATER_LOADS)
            pe.wait_ge(x_ready, NT)
            for n in range(1, len(GROUPS)):
                transpose_weights(n)
            pe.wait_ge(w_ready, len(GROUPS))
            pe.wait_ge(table_evac, NBLK)
            all_steps(0)
            for j in range(NT):
                pe.wait_ge(acts_ready, TILES if j >= 4 else TILES - 1)
                for m, (w, part) in enumerate(PARTS):
                    nc.tensor.matmul(ps[:, j, :], w[:, 0, WLR, C:2 * C], x_split[:, part, tl(j)],
                                     start=m == 0, stop=False)
                pe.wait_ge(h_ready, TILES - NT + j + 1)
                for m, (w, part) in enumerate(PARTS):
                    last = nc.tensor.matmul(ps[:, j, :], w[:, 0, WLR, 0:C], (h_hi, h_lo)[part][:, tl(j)],
                                            start=False, stop=m == 2)
                last.then_inc(lin_ready, 1)
                if j > 0:
                    h1_by_rows(j - 1)
            h1_by_rows(NT - 1)
            pe.wait_ge(h1_rows_ready, 4)
            for k in range(NT):
                pe.wait_ge(h1_ready, k + 1)
                table_rows(1, k, h1_split, 0)
            pe.wait_ge(table_evac, 2 * NBLK)
            pe.wait_ge(h1_rows_ready, NT)
            all_steps(1)
            for k in range(NT):
                pe.wait_ge(acts_ready, 2 * TILES if k >= 4 else 2 * TILES - 1)
                pe.wait_ge(h_ready, 2 * TILES - NT + k + 1)
                for b in range(BPT):
                    n = k * BPT + b
                    for m, (w, part) in enumerate(PARTS):
                        nc.tensor.matmul(ps[:, k, blk(b)], h1_split[:, part, blk(n)], w[:, 1, WLR, C:2 * C],
                                         start=m == 0, stop=False, skip_group_check=True)
                    for m, (w, part) in enumerate(PARTS):
                        last = nc.tensor.matmul(ps[:, k, blk(b)], (h_hi, h_lo)[part][:, blk(n)],
                                                w[:, 1, WLR, 0:C],
                                                start=False, stop=m == 2, skip_group_check=True)
                last.then_inc(out_psum, 1)

        @block.scalar
        def _(act):
            load_w(act, 0, 0, NQ, wih, wih_loaded)
            load_b(act, 0, first_b_loaded)
            def weights_high(n):
                layer, group = GROUPS[n]
                act.wait_ge(w_transposed, n + 1)
                for cols, scale in w_pieces(group):
                    last = nc.scalar.mul(w_hi[:, layer, group, cols], ps[:, n % 4, cols], scale)
                last.then_inc(w_hi_ready, 1)

            weights_high(0)
            for k in range(NT):
                act.wait_ge(xT_psum, k + 1)
                nc.scalar.copy(x_split[:, 0, tl(k)], ps[:, 2 + k % 2, :]).then_inc(x_hi_ready, 1)
            for n in range(1, len(GROUPS)):
                weights_high(n)

            def tanh_c(tile, j, reused=True):
                act.wait_ge(c_ready, tile + 1)
                if reused:
                    act.wait_ge(h32_ready, tile - 1)
                nc.scalar.activation(tanc[:, j % 2, :], cg[:, j, :], ACT.Tanh).then_inc(tanc_ready, 1)

            def act_first(layer):
                act.wait_ge(biasT_ready, layer + 1)
                for what, j in FIRST_ORDER[layer]:
                    if what == "T":
                        act.wait_ge(inT_psum, layer * NT + j + 1)
                        nc.scalar.copy(h_hi[:, tl(j)], ps[:, T_BANK[layer][j], :]).then_inc(in_hi, 1)
                        continue
                    tile = layer * TILES + j
                    bank = j % 2 * NQ
                    act.wait_ge(gates_ready, tile + 1)
                    if layer > 0 or j >= SIGSLOTS:
                        act.wait_ge(h32_ready, tile - SIGSLOTS + 1)
                    if layer > 0 or j >= 2:
                        act.wait_ge(c_ready, tile - 1)
                    for k, q in enumerate(GATE):
                        to = sig[:, j % SIGSLOTS, k, :] if k < 3 else cg[:, NT + j % 2, :]
                        last = nc.scalar.activation(to, ps[:, bank + k, :], ACT.Sigmoid if k < 3 else ACT.Tanh,
                                                    bias=biasT[:, layer, q:q + 1], scale=1.0 / Z_SCALE)
                        if k == 0:
                            last.then_inc(first_gate_read, 1)
                    last.then_inc(acts_ready, 1)
                    if j > 0:
                        tanh_c(tile - 1, j - 1, layer > 0 or j > 2)

            def act_step(layer, t):
                for j in range(NT):
                    tile = layer * TILES + t * NT + j
                    bank = j % 2 * NQ
                    act.wait_ge(gates_ready, tile + 1)
                    act.wait_ge(h32_ready, tile - SIGSLOTS + 1)
                    act.wait_ge(c_ready, tile - 1)
                    nc.scalar.activation(sig[:, j % SIGSLOTS, :, :], ps[:, bank:bank + 3, :], ACT.Sigmoid,
                                         scale=1.0 / Z_SCALE)
                    nc.scalar.activation(cg[:, NT + j % 2, :], ps[:, bank + 3, :], ACT.Tanh,
                                         scale=1.0 / Z_SCALE).then_inc(acts_ready, 1)
                    tanh_c(tile - 1, (j - 1) % NT)

            def all_steps(layer):
                act_first(layer)
                with act.Fori(1, DEG) as t:
                    act_step(layer, t)
                tanh_c((layer + 1) * TILES - 1, NT - 1)

            all_steps(0)
            for j in range(NT):
                act.wait_ge(lin_ready, j + 1)
                if j >= 2:
                    act.wait_ge(h1_ready, j - 1)
                    act.wait_ge(h1_rows_psum, j - 1)
                nc.scalar.activation(h1_tmp[:, j % 2, :], ps[:, j, :], ACT.Relu, bias=bl1[:, :],
                                     scale=1.0 / Z_SCALE).then_inc(h1_relu, 1)
                act.wait_ge(h1_relu, j + 1)
                nc.scalar.copy(h1_split[:, 0, tl(j)], h1_tmp[:, j % 2, :]).then_inc(h1_hi, 1)
            all_steps(1)
            def normalise(k):
                act.wait_ge(shift_ready, k + 1)
                for b in range(k * BPT, (k + 1) * BPT):
                    nc.scalar.activation(y[:, b, :], y[:, b, :], ACT.Identity, bias=shift[:, b:b + 1],
                                         scale=rstd[:, b:b + 1]).then_inc(y_ready, 1)

            for k in range(NT):
                bs = slice(k * BPT, (k + 1) * BPT)
                act.wait_ge(mv_ready, (k + 1) * BPT)
                nc.scalar.activation(std[:, bs], mv[:, bs, 1], ACT.Sqrt, bias=epst[:, :]).then_inc(std_ready, 1)
                if k > 0:
                    normalise(k - 1)
            normalise(NT - 1)

        @block.vector
        def _(dve):
            nc.vector.memset(epst[:, :], EPS).then_inc(eps_ready, 1)

            def make_bias(layer):
                for k, q in enumerate(GATE):
                    nc.vector.tensor_tensor(b_sum[:, layer, blk(k)], b_in[:, layer, 0, blk(q)],
                                            b_in[:, layer, 1, blk(q)], ALU.add).then_inc(b_summed, 1)
                dve.wait_ge(b_summed, (layer + 1) * NQ)
                nc.vector.tensor_scalar(bias[:, layer, :], b_sum[:, layer, :], Z_SCALE, None, ALU.mult
                                        ).then_inc(bias_ready, 1)

            def split_weights(n):
                layer, group = GROUPS[n]
                dve.wait_ge(w_hi_ready, n + 1)
                for cols, scale in w_pieces(group):
                    last = nc.vector.scalar_tensor_tensor(w_lo[:, layer, group, cols], ps[:, n % 4, cols], scale,
                                                          w_hi[:, layer, group, cols], ALU.mult, ALU.subtract)
                last.then_inc(w_ready, 1)

            def x_low(k):
                dve.wait_ge(x_hi_ready, k + 1)
                nc.vector.tensor_tensor(x_split[:, 1, tl(k)], ps[:, 2 + k % 2, :], x_split[:, 0, tl(k)],
                                        ALU.subtract).then_inc(x_ready, 1)

            def table_rows(layer, k, bank):
                n = layer * NT + k
                if n >= ROWSLOTS:
                    dve.wait_ge(table_stored[n % ROWSLOTS], 2 * 16 * (n // ROWSLOTS))
                for b in range(n * BPT, (n + 1) * BPT):
                    dve.wait_ge(table_psum, b + 1)
                    nc.vector.tensor_tensor(rows[:, n % ROWSLOTS, b % BPT, :], ps[:, bank + b % 4, :],
                                            bias[:, layer, :], ALU.add).then_inc(table_evac, 1)

            def h_start(tile, j):
                dve.wait_ge(tanc_ready, tile + 1)
                nc.vector.scalar_tensor_tensor(h32[:, j % 2, :], sig[:, j % SIGSLOTS, 2, :], H_SCALE, tanc[:, j % 2, :],
                                               ALU.mult, ALU.mult).then_inc(h32_ready, 1)

            def h_split(tile, j):
                dve.wait_ge(h32_ready, tile + 1)
                nc.vector.tensor_copy(h_hi[:, tl(j)], h32[:, j % 2, :]).then_inc(hi_ready, 1)
                dve.wait_ge(hi_ready, tile + 1)
                nc.vector.tensor_tensor(h_lo[:, tl(j)], h32[:, j % 2, :], h_hi[:, tl(j)], ALU.subtract
                                        ).then_inc(h_ready, 1)

            def state_first(layer):
                for what, j in FIRST_ORDER[layer]:
                    if what == "T":
                        dve.wait_ge(in_hi, layer * NT + j + 1)
                        nc.vector.tensor_tensor(h_lo[:, tl(j)], ps[:, T_BANK[layer][j], :], h_hi[:, tl(j)], ALU.subtract
                                                ).then_inc(in_split, 1)
                        continue
                    tile = layer * TILES + j
                    dve.wait_ge(acts_ready, tile + 1)
                    nc.vector.tensor_tensor(cg[:, j, :], sig[:, j % SIGSLOTS, 1, :], cg[:, NT + j % 2, :], ALU.mult
                                            ).then_inc(c_ready, 1)
                    if j > 0:
                        h_start(tile - 1, j - 1)
                        h_split(tile - 1, j - 1)

            def state_step(layer, t):
                for j in range(NT):
                    tile = layer * TILES + t * NT + j
                    g = NT + j % 2
                    dve.wait_ge(acts_ready, tile + 1)
                    nc.vector.tensor_tensor(prod[:, j % 2, :, :], sig[:, j % SIGSLOTS, 0:2, :],
                                            cg[:, j:g + 1:g - j, :], ALU.mult).then_inc(prod_ready, 1)
                    h_start(tile - 1, (j - 1) % NT)
                    dve.wait_ge(prod_ready, tile + 1 - NT * (layer + 1))
                    nc.vector.tensor_tensor(cg[:, j, :], prod[:, j % 2, 0, :], prod[:, j % 2, 1, :], ALU.add
                                            ).then_inc(c_ready, 1)
                    nc.vector.tensor_copy(stage[:, j, :], idx[:, j * BPT:(j + 1) * BPT, t + 1]).then_inc(staged, 1)
                    h_split(tile - 1, (j - 1) % NT)

            def all_steps(layer):
                state_first(layer)
                with dve.Fori(1, DEG) as t:
                    state_step(layer, t)
                h_start((layer + 1) * TILES - 1, NT - 1)
                h_split((layer + 1) * TILES - 1, NT - 1)

            def h1_to_rows(j):
                dve.wait_ge(h1_rows_psum, j + 1)
                if j >= H1SLOTS:
                    dve.wait_ge(h1_stored[j % H1SLOTS], 16 * (j // H1SLOTS))
                nc.vector.tensor_copy(h1_out[:, j % H1SLOTS, :], ps[:, j, :]).then_inc(h1_rows_ready, 1)

            split_weights(0)
            x_low(0)
            x_low(1)
            dve.wait_ge(first_b_loaded, 2 * 16)
            make_bias(0)
            dve.wait_ge(bias_ready, 1)
            for k in range(NT):
                table_rows(0, k, 4)
                if k + 2 < NT:
                    x_low(k + 2)
                if k == 4:
                    dve.wait_ge(idx0_loaded, 16)
                    dve.wait_ge(idx_loaded, 16)
                    nc.vector.tensor_copy(stage[:, :, :].rearrange("p j b -> p (j b)"), idx[:, :, 1]
                                          ).then_inc(staged, NT)
                    nc.vector.tensor_copy(idx[:, :, DEG], idx[:, :, 1]).then_inc(idx_wrapped, 1)
            for n in range(1, len(GROUPS)):
                split_weights(n)
            dve.wait_ge(later_loaded, 16 * LATER_LOADS)
            make_bias(1)
            for layer in range(LAYERS):
                nc.vector.tensor_tensor(biasT[:, layer, :], bT_in[:, layer, 0, :], bT_in[:, layer, 1, :], ALU.add
                                        ).then_inc(biasT_ready, 1)
            dve.wait_ge(bias_ready, 2)
            dve.wait_ge(idx_wrapped, 1)
            all_steps(0)
            for j in range(NT):
                dve.wait_ge(h1_hi, j + 1)
                nc.vector.tensor_tensor(h1_split[:, 1, tl(j)], h1_tmp[:, j % 2, :], h1_split[:, 0, tl(j)],
                                        ALU.subtract).then_inc(h1_ready, 1)
                if j > 0:
                    h1_to_rows(j - 1)
            h1_to_rows(NT - 1)
            for k in range(NT):
                table_rows(1, k, 0)
            all_steps(1)

            def scales(k):
                bs = slice(k * BPT, (k + 1) * BPT)
                dve.wait_ge(std_ready, k + 1)
                nc.vector.reciprocal(rstd[:, bs], std[:, bs]).then_inc(rstd_ready, 1)
                dve.wait_ge(rstd_ready, k + 1)
                nc.vector.scalar_tensor_tensor(shift[:, bs], mv[:, bs, 0], -1.0, rstd[:, bs], ALU.mult, ALU.mult
                                               ).then_inc(shift_ready, 1)

            for k in range(NT):
                bs = slice(k * BPT, (k + 1) * BPT)
                dve.wait_ge(out_psum, k + 1)
                dve.wait_ge(xres_ready, k + 1)
                nc.vector.scalar_tensor_tensor(y[:, bs, :], ps[:, k, :].rearrange("p (b c) -> p b c", c=C),
                                               1.0 / Z_SCALE, x_in[:, bs, :], ALU.mult, ALU.add).then_inc(y_sum, 1)
                dve.wait_ge(y_sum, k + 1)
                for b in range(k * BPT, (k + 1) * BPT):
                    nc.vector.bn_stats(stats[:, b, :], y[:, b, :]).then_inc(stats_ready, 1)
                if k > 0:
                    scales(k - 1)
                for b in range(k * BPT, (k + 1) * BPT):
                    dve.wait_ge(stats_ready, b + 1)
                    nc.vector.bn_aggr(mv[:, b, :], stats[:, b, :]).then_inc(mv_ready, 1)
            scales(NT - 1)


_WEIGHTS = ["wih", "whh", "bih", "bhh", "wl", "bl", "wr"]


def kernel(**inputs):
    import numpy as np
    import concourse.bacc as bacc
    from concourse import mybir as mb
    from concourse.bass_utils import run_bass_kernel_spmd

    nc = bacc.Bacc("TRN2", target_bir_lowering=False, num_devices=1)
    arrays = {}

    def given(name):
        a = np.ascontiguousarray(inputs[name])
        arrays[f"in_{name}"] = a
        return nc.dram_tensor(f"in_{name}", a.shape, mb.dt.from_np(a.dtype), kind="ExternalInput").ap()

    x, src = given("x"), given("src")
    layers = [[given(f"L0_gnn_conv{i}_{w}") for w in _WEIGHTS] for i in (1, 2)]
    shape = inputs["x"].shape
    table = [nc.dram_tensor(f"table{i}", (shape[0], 4 * shape[1]), mb.dt.float32, kind="Internal").ap()
             for i in (1, 2)]
    out = nc.dram_tensor("out", shape, mb.dt.float32, kind="ExternalOutput").ap()
    h1_rows = nc.dram_tensor("h1_rows", shape, mb.dt.float32, kind="Internal").ap()
    sage_lstm_resnorm_kernel(nc, x, src, layers, table, h1_rows, out)
    r = run_bass_kernel_spmd(nc, [arrays], core_ids=[0])
    return r.results[0]["out"]
```
